# Optimizing a Trainium2 kernel written in Bass

```python
import numpy as np
import jax
import jax.numpy as jnp

def _softmax(x, axis=-1):
    return jax.nn.softmax(x, axis=axis)

def _gelu(x):
    return jax.nn.gelu(x, approximate=True)

def _silu(x):
    return jax.nn.silu(x)

def _sigmoid(x):
    return jax.nn.sigmoid(x)

def _layernorm(x, axis=-1, eps=1e-05):
    m = jnp.mean(x, axis=axis, keepdims=True)
    v = jnp.var(x, axis=axis, keepdims=True)
    return (x - m) / jnp.sqrt(v + eps)

def _scatter_add(tgt, idx, src, axis=0):
    return tgt.at[idx].add(src)

def _segment_sum(src, seg, n):
    return jax.ops.segment_sum(src, seg, n)
kernel_name = 'mk_adaln_ffn_d1_seqx_r8_412954'

def setup_inputs(seed: int=0):
    np.random.seed(seed)
    _w = jnp.asarray

    def _rec_inputs():
        import jax
        import jax.numpy as jnp
        _rk = jax.random.key(seed)
        x = -7.109e-05 + 0.9999 * jax.random.normal(jax.random.fold_in(_rk, 1), (64, 32, 256), jnp.float32)
        _lenS = 32 - jax.random.randint(jax.random.fold_in(_rk, 7), (64,), 0, max(1, 32 // 4) + 1, jnp.int32)
        _lenS2 = 32 - jax.random.randint(jax.random.fold_in(_rk, 8), (64,), 0, max(1, 32 // 4) + 1, jnp.int32)
        itok_B_1_198 = jax.random.randint(jax.random.fold_in(_rk, 11), (64,), 1, 199, jnp.int32)
        return (x, itok_B_1_198)
    x, itok_B_1_198 = _rec_inputs()

    def _L0_cond_setup():
        import jax, jax.numpy as jnp
        import numpy as np
        B, C, T = (128, 32, 256)
        S, D = (200, 32)
        key = jax.random.key(seed)
        k1, k2, k3 = jax.random.split(key, 3)
        x = jax.random.normal(k1, (B, C, T), dtype=jnp.float32)
        conditions = jax.random.randint(k2, (B,), 0, S, dtype=jnp.int64)
        weights = jax.random.normal(k3, (S, C, D), dtype=jnp.float32) / jnp.sqrt(jnp.float32(C))
        return {'x': x, 'conditions': conditions, 'weights': weights}
    _L0_cond_all = _L0_cond_setup()
    _L0_cond_in = {k: v for k, v in _L0_cond_all.items() if k in ('weights',)}
    del _L0_cond_all

    def _L0_ffn_setup():
        import jax, jax.numpy as jnp
        import numpy as np
        H = 256
        I = 176
        E = 8
        K = 2
        B, S = (2, 256)
        key = jax.random.key(seed)
        k0, k1, k2, k3, k4 = jax.random.split(key, 5)
        scale = 1.0 / np.sqrt(H)
        x = jax.random.normal(k0, (B, S, H), dtype=jnp.float32)
        Wr = jax.random.normal(k1, (H, E), dtype=jnp.float32) * scale
        Wg = jax.random.normal(k2, (E, H, I), dtype=jnp.float32) * scale
        Wu = jax.random.normal(k3, (E, H, I), dtype=jnp.float32) * scale
        Wd = jax.random.normal(k4, (E, I, H), dtype=jnp.float32) * (1.0 / np.sqrt(I))
        return {'x': x, 'Wr': Wr, 'Wg': Wg, 'Wu': Wu, 'Wd': Wd}
    _L0_ffn_all = _L0_ffn_setup()
    _L0_ffn_in = {k: v for k, v in _L0_ffn_all.items() if k in ('Wr', 'Wg', 'Wu', 'Wd')}
    del _L0_ffn_all
    return {'x': x, 'itok_B_1_198': itok_B_1_198, 'L0_cond_weights': _L0_cond_in['weights'], 'L0_ffn_Wr': _L0_ffn_in['Wr'], 'L0_ffn_Wg': _L0_ffn_in['Wg'], 'L0_ffn_Wu': _L0_ffn_in['Wu'], 'L0_ffn_Wd': _L0_ffn_in['Wd']}

def reference(x, itok_B_1_198, L0_cond_weights, L0_ffn_Wr, L0_ffn_Wg, L0_ffn_Wu, L0_ffn_Wd):
    import jax
    import jax.numpy as jnp

    def _L0_cond_ref(x, conditions, weights):
        import jax, jax.numpy as jnp
        import numpy as np
        B, C, T = (128, 32, 256)
        S, D = (200, 32)
        w = weights[conditions]
        return jnp.einsum('bct,bcd->bdt', x, w)

    def _L0_ffn_ref(x, Wr, Wg, Wu, Wd):
        import jax, jax.numpy as jnp
        import numpy as np
        H = 256
        I = 176
        E = 8
        K = 2
        B, S = (2, 256)
        router_logits = jnp.einsum('bsh,he->bse', x, Wr)
        probs = jax.nn.softmax(router_logits.astype(jnp.float32), axis=-1)
        topk_w, topk_idx = jax.lax.top_k(probs, K)
        topk_w = topk_w / jnp.sum(topk_w, axis=-1, keepdims=True)
        onehot = jax.nn.one_hot(topk_idx, E, dtype=topk_w.dtype)
        combine = jnp.einsum('bsk,bske->bse', topk_w, onehot)
        g = jnp.einsum('bsh,ehi->besi', x, Wg)
        u = jnp.einsum('bsh,ehi->besi', x, Wu)
        h = jax.nn.silu(g) * u
        y = jnp.einsum('besi,eih->besh', h, Wd)
        out = jnp.einsum('bse,besh->bsh', combine.astype(x.dtype), y)
        return out
    x = x + _L0_ffn_ref(_L0_cond_ref(x, itok_B_1_198, L0_cond_weights), L0_ffn_Wr, L0_ffn_Wg, L0_ffn_Wu, L0_ffn_Wd)
    return x

_drawn_inputs = setup_inputs


def setup_inputs(seed=0):
    import zlib

    import numpy as np

    out = dict(_drawn_inputs(seed))
    spreads = {}
    factors = {}
    for name, (base, spread) in spreads.items():
        noise = np.random.default_rng([zlib.crc32(name.encode()), seed]).standard_normal(out[name].shape)
        drawn = base * np.exp(spread * noise) if base else spread * noise
        out[name] = jnp.asarray(drawn.astype(out[name].dtype))
    for name, factor in factors.items():
        out[name] = (out[name] * factor).astype(out[name].dtype)
    return out
```

```python
from contextlib import ExitStack

import concourse.bass as bass
from concourse import mybir

ALU = mybir.AluOpType
ACT = mybir.ActivationFunctionType
AX_X = mybir.AxisListType.X
F32 = mybir.dt.float32
F32R = mybir.dt.float32r
I32 = mybir.dt.int32

P = 128
DMA = 16


def adaln_ffn_kernel(nc, x, token_id, cond_w, w_router, w_gate, w_up, w_down, out):
    B, C, H = x.shape
    S, _, D = cond_w.shape
    E, _, I = w_gate.shape
    TOK = B * D
    F = E * I
    FT = F // P
    KT = H // P
    NT = 512
    CH = TOK // NT
    G = TOK // P
    GC = NT // P
    Q = P // C
    assert C == D == 32 and F % P == 0 and H % P == 0 and TOK % NT == 0 and E == 8

    WP = 4
    EP = E // WP
    PF = EP * I
    STAGE = 3
    DT = 3
    DP = -(-FT // DT)
    DSTAGE = 2
    HS = 4
    LAG = 2

    x_v = x.rearrange("(g q) c t -> (q c) g t", q=Q)
    out_v = out.rearrange("(g q) c t -> (q c) g t", q=Q)
    cond_rows = cond_w.rearrange("s c d -> (s c) d")
    wr_v = w_router.rearrange("(k p) e -> p k e", p=P)
    wd_v = w_down.rearrange("e i h -> (e i) h").rearrange("(j p) h -> p j h", p=P)
    comb_dram = nc.dram_tensor("comb_dram", [E * G, P], F32, kind="Internal").ap()
    comb_rows = comb_dram.rearrange("(e g) p -> e (g p)", e=E)

    expert_rows = []
    for j in range(FT):
        rows = []
        for e in range(j * P // I, (j * P + P - 1) // I + 1):
            rows.append((e, max(e * I - j * P, 0), min((e + 1) * I - j * P, P)))
        expert_rows.append(rows)

    def piece_of(j):
        return (j * P + P - 1) // PF

    with ExitStack() as ctx:
        def sb(name, shape, dt=F32):
            return ctx.enter_context(nc.sbuf_tensor(name, shape, dt))

        def bank(name):
            return ctx.enter_context(nc.psum_tensor(name, [P, NT], F32))

        def sem(name):
            return ctx.enter_context(nc.semaphore(name))

        x_sb = sb("x_sb", [P, G, H])
        ids = sb("ids", [P, B], I32)
        ids_f = sb("ids_f", [P, B])
        chan = sb("chan", [P, 1], I32)
        chan_f = sb("chan_f", [P, 1])
        row_idx = sb("row_idx", [P, G], I32)
        cond_sb = sb("cond_sb", [P, G, D])
        cond_diag = sb("cond_diag", [P, G, Q, D])
        z_hi = sb("z_hi", [P, KT, TOK], F32R)
        z_lo = sb("z_lo", [P, KT, TOK], F32R)
        wr_stage = sb("wr_stage", [P, KT, E])
        wr_parts = sb("wr_parts", [P, KT, 2 * E], F32R)
        gu_stage = sb("gu_stage", [P, STAGE, 2, KT, PF])
        d_stage = sb("d_stage", [P, DSTAGE, DT, H])
        wg_hi = sb("wg_hi", [P, KT, F], F32R)
        wg_lo = sb("wg_lo", [P, KT, F], F32R)
        wu_hi = sb("wu_hi", [P, KT, F], F32R)
        wu_lo = sb("wu_lo", [P, KT, F], F32R)
        wd_hi = sb("wd_hi", [P, FT, H], F32R)
        wd_lo = sb("wd_lo", [P, FT, H], F32R)
        ident = sb("ident", [P, P])
        rank = sb("rank", [P, E])
        logit = sb("logit", [P, G, 2 * E])
        prob = sb("prob", [P, G, E])
        pick = sb("pick", [P, G, E])
        first = sb("first", [P, G, E])
        left = sb("left", [P, G, E])
        best = sb("best", [P, 6, G])
        comb = sb("comb", [P, E, G])
        comb_t = sb("comb_t", [P, P])
        comb_bc = sb("comb_bc", [P, FT, NT])
        silu_g = sb("silu_g", [P, 2, NT])
        hid = sb("hid", [P, 2, NT])
        hid_hi = sb("hid_hi", [P, HS, NT], F32R)
        hid_lo = sb("hid_lo", [P, HS, NT], F32R)
        out_t = sb("out_t", [P, KT, NT])

        ps_g = [bank("ps_g0"), bank("ps_g1")]
        ps_u = [bank("ps_u0"), bank("ps_u1")]
        ps_o = [bank("ps_o0"), bank("ps_o1")]
        ps_s = [bank("ps_s0"), bank("ps_s1")]
        gate_bank = [ps_s[0] if j == FT - 1 else ps_g[j % 2] for j in range(FT)]
        up_bank = [ps_s[1] if j == FT - 1 else ps_u[j % 2] for j in range(FT)]
        z_bank = [ps_g[0], ps_g[1], ps_u[0], ps_u[1]]

        ids_in = sem("ids_in")
        x_in = [sem(f"x_in{c}") for c in range(CH)]
        wr_in = sem("wr_in")
        gu_in = [sem(f"gu_in{w}") for w in range(WP)]
        d_in = [sem(f"d_in{w}") for w in range(DP)]
        cond_in = [sem(f"cond_in{c}") for c in range(CH)]
        comb_out = sem("comb_out")
        comb_in = [sem(f"comb_in{j}") for j in range(FT)]
        stored = sem("stored")
        consts = sem("consts")
        idx_step = sem("idx_step")
        diag_done = sem("diag_done")
        z_ready = sem("z_ready")
        z_hi_done = sem("z_hi_done")
        z_lo_done = sem("z_lo_done")
        wr_hi_done = sem("wr_hi_done")
        wr_done = sem("wr_done")
        gu_hi_done = sem("gu_hi_done")
        gu_lo_done = sem("gu_lo_done")
        d_hi_done = sem("d_hi_done")
        d_lo_done = sem("d_lo_done")
        logit_ready = sem("logit_ready")
        route = sem("route")
        exp_done = sem("exp_done")
        comb_ready = sem("comb_ready")
        comb_t_ready = sem("comb_t_ready")
        comb_t_done = sem("comb_t_done")
        gate_ready = sem("gate_ready")
        up_ready = sem("up_ready")
        silu_done = sem("silu_done")
        su_done = sem("su_done")
        hid_done = sem("hid_done")
        hi_done = sem("hi_done")
        lo_done = sem("lo_done")
        down_done = sem("down_done")
        out_t_done = sem("out_t_done")
        tr_ready = sem("tr_ready")
        add_done = sem("add_done")

        def dist(slot_of, j):
            d = 1
            while slot_of((j - d) % FT) != slot_of(j):
                d += 1
            return d

        def bank_of(j):
            return 2 if j == FT - 1 else j % 2

        def wait_tile(eng, semaphore, c, j):
            if isinstance(c, int):
                if c * FT + j + 1 <= 0:
                    return
            eng.wait_ge(semaphore, c * FT + (j + 1))

        block = ctx.enter_context(nc.Block())

        @block.sync
        def _(sp):
            sp.dma_start(ids[:, :], token_id.rearrange("(a b) -> a b", a=1).broadcast_to((P, B))
                         ).then_inc(ids_in, DMA)
            sp.dma_start(wr_stage[:, :, :], wr_v).then_inc(wr_in, DMA)
            for c in range(CH):
                sp.dma_start(x_sb[:, c * GC:(c + 1) * GC, :], x_v[:, c * GC:(c + 1) * GC, :]
                             ).then_inc(x_in[c], DMA)

            def load_gate_up(w):
                if w >= STAGE:
                    sp.wait_ge(gu_hi_done, w - STAGE + 1)
                    sp.wait_ge(gu_lo_done, w - STAGE + 1)
                for n, src in enumerate((w_gate, w_up)):
                    for k in range(KT):
                        dst = gu_stage[:, w % STAGE, n, k, :].rearrange("p (e i) -> p e i", e=EP)
                        sp.dma_start(dst, src[w * EP:(w + 1) * EP, k * P:(k + 1) * P, :]
                                     .rearrange("e p i -> p e i")).then_inc(gu_in[w], DMA)

            def load_down(w):
                if w >= DSTAGE:
                    sp.wait_ge(d_hi_done, w - DSTAGE + 1)
                    sp.wait_ge(d_lo_done, w - DSTAGE + 1)
                n = min(DT, FT - w * DT)
                sp.dma_start(d_stage[:, w % DSTAGE, 0:n, :], wd_v[:, w * DT:w * DT + n, :]
                             ).then_inc(d_in[w], DMA)

            load_gate_up(0)
            load_down(0)
            load_gate_up(1)
            load_gate_up(2)
            load_down(1)

            def broadcast_comb(c, j):
                for e, lo, hi in expert_rows[j]:
                    sp.dma_start(comb_bc[lo:hi, j, :],
                                 comb_rows[e:e + 1, bass.ts(c, NT)].broadcast_to((hi - lo, NT))
                                 ).then_inc(comb_in[j], DMA)

            sp.wait_ge(comb_t_done, 1)
            sp.dma_start(comb_dram, comb_t[:, :]).then_inc(comb_out, DMA)
            sp.wait_ge(comb_out, DMA)
            for j in range(FT):
                broadcast_comb(0, j)
            load_gate_up(3)
            load_down(2)
            load_down(3)
            with sp.Fori(1, CH) as c:
                for j in range(FT):
                    wait_tile(sp, hid_done, c - 1, j)
                    broadcast_comb(c, j)

        @block.gpsimd
        def _(pool):
            pool.iota(chan[:, :], pattern=[[0, 1]], base=0, channel_multiplier=1).then_inc(consts, 1)
            pool.memset(cond_diag[:, :, :, :], 0.0).then_inc(consts, 1)
            pool.memset(ident[:, :], 0.0).then_inc(consts, 1)
            for e in range(E):
                pool.memset(rank[:, e:e + 1], float(E - e)).then_inc(consts, 1)
            pool.wait_ge(idx_step, 5)
            for g in range(G):
                pool.indirect_dma_start(
                    out=cond_sb[:, g, :], out_offset=None, in_=cond_rows,
                    in_offset=bass.IndirectOffsetOnAxis(ap=row_idx[:, g:g + 1], axis=0),
                ).then_inc(cond_in[g // GC], DMA)
            pool.wait_ge(consts, 3)
            pool.affine_select(out=ident[:, :], in_=ident[:, :], compare_op=ALU.not_equal, fill=1.0,
                               base=0, pattern=[[-1, P]], channel_multiplier=1).then_inc(consts, 1)

            def low_parts_gate_up(w):
                pool.wait_ge(gu_hi_done, w + 1)
                for n, (hi, lo) in enumerate(((wg_hi, wg_lo), (wu_hi, wu_lo))):
                    s = slice(w * PF, (w + 1) * PF)
                    last = pool.tensor_tensor(lo[:, :, s], gu_stage[:, w % STAGE, n, :, :],
                                              hi[:, :, s].bitcast(F32), ALU.subtract)
                last.then_inc(gu_lo_done, 1)

            def low_parts_down(w):
                n = min(DT, FT - w * DT)
                pool.wait_ge(d_hi_done, w + 1)
                s = slice(w * DT, w * DT + n)
                pool.tensor_tensor(wd_lo[:, s, :], d_stage[:, w % DSTAGE, 0:n, :],
                                   wd_hi[:, s, :].bitcast(F32), ALU.subtract).then_inc(d_lo_done, 1)

            for w in range(WP):
                low_parts_gate_up(w)
                low_parts_down(w)

        @block.scalar
        def _(act):
            act.wait_ge(wr_in, DMA)
            act.activation(wr_parts[:, :, 0:E], wr_stage[:, :, :], ACT.Copy).then_inc(wr_hi_done, 1)
            for n in range(CH * KT):
                c, k = divmod(n, KT)
                act.wait_ge(z_ready, n + 1)
                act.activation(z_hi[:, k, c * NT:(c + 1) * NT], z_bank[n % 4][:, :], ACT.Copy
                               ).then_inc(z_hi_done, 1)

            def high_parts_gate_up(w):
                act.wait_ge(gu_in[w], 2 * KT * DMA)
                for n, hi in enumerate((wg_hi, wu_hi)):
                    last = act.activation(hi[:, :, w * PF:(w + 1) * PF], gu_stage[:, w % STAGE, n, :, :],
                                          ACT.Copy)
                last.then_inc(gu_hi_done, 1)

            def high_parts_down(w):
                n = min(DT, FT - w * DT)
                act.wait_ge(d_in[w], DMA)
                act.activation(wd_hi[:, w * DT:w * DT + n, :], d_stage[:, w % DSTAGE, 0:n, :],
                               ACT.Copy).then_inc(d_hi_done, 1)

            high_parts_gate_up(0)
            act.wait_ge(logit_ready, 1)
            act.activation(logit[:, :, :], ps_s[0][:, 0:G * 2 * E].rearrange("p (g e) -> p g e", g=G),
                           ACT.Copy).then_inc(exp_done, 1)
            high_parts_down(0)
            act.wait_ge(route, 3)
            act.activation(prob[:, :, :], left[:, :, :], ACT.Exp).then_inc(exp_done, 1)
            high_parts_gate_up(1)
            act.wait_ge(comb_t_ready, 1)
            act.activation(comb_t[:, :], ps_s[1][:, 0:P], ACT.Copy).then_inc(comb_t_done, 1)

            def activate(c, j):
                wait_tile(act, gate_ready, c, j)
                wait_tile(act, su_done, c, j - dist(lambda i: i % 2, j))
                act.activation(silu_g[:, j % 2, :], gate_bank[j][:, :], ACT.Silu).then_inc(silu_done, 1)

            def split_high(c, j):
                wait_tile(act, hid_done, c, j)
                wait_tile(act, down_done, c, j - dist(lambda i: i % HS, j))
                act.activation(hid_hi[:, j % HS, :], hid[:, j % 2, :], ACT.Copy).then_inc(hi_done, 1)

            def evacuate(c):
                wait_tile(act, down_done, c, FT - 1)
                act.wait_ge(tr_ready, 2 * c) if not isinstance(c, int) or c > 0 else None
                for k in range(KT):
                    act.activation(out_t[:, k, :], ps_o[k][:, :], ACT.Copy).then_inc(out_t_done, 1)

            def store(c):
                act.wait_ge(add_done, 2 * c + 2)
                act.dma_start(out_v[:, bass.ts(c, GC), :], x_sb[:, bass.ts(c, GC), :]).then_inc(stored, DMA)

            for j in range(FT):
                activate(0, j)
                split_high(0, j)
                if j == 0:
                    high_parts_gate_up(2)
                if j == 1:
                    high_parts_down(1)
                if j == 3:
                    high_parts_gate_up(3)
                if j == 4:
                    high_parts_down(2)
                if j == 6:
                    high_parts_down(3)
            with act.Fori(1, CH) as c:
                for j in range(FT):
                    activate(c, j)
                    if j == LAG:
                        evacuate(c - 1)
                    split_high(c, j)
                    if j == 6:
                        store(c - 1)
            evacuate(CH - 1)
            store(CH - 1)
            act.wait_ge(stored, CH * DMA)

        @block.vector
        def _(dve):
            dve.wait_ge(ids_in, DMA)
            dve.tensor_scalar(ids_f[:, :], ids[:, :], 0.0, float(S - 1), ALU.max, ALU.min).then_inc(idx_step, 1)
            dve.wait_ge(consts, 1)
            dve.tensor_copy(chan_f[:, :], chan[:, :]).then_inc(idx_step, 1)
            dve.wait_ge(idx_step, 2)
            for q in range(1, Q):
                s = slice(q * C, (q + 1) * C)
                last = dve.tensor_scalar(chan_f[s, :], chan_f[s, :], float(-q * C), None, ALU.add)
            last.then_inc(idx_step, 1)
            dve.wait_ge(idx_step, 3)
            ids_v = ids_f[:, :].rearrange("p (g q) -> p q g", q=Q)
            for q in range(Q):
                s = slice(q * C, (q + 1) * C)
                last = dve.tensor_scalar(row_idx[s, :], ids_v[s, q, :], float(C), chan_f[s, 0:1],
                                         ALU.mult, ALU.add)
            last.then_inc(idx_step, 2)
            dve.wait_ge(wr_hi_done, 1)
            dve.tensor_tensor(wr_parts[:, :, E:2 * E], wr_stage[:, :, :],
                              wr_parts[:, :, 0:E].bitcast(F32), ALU.subtract).then_inc(wr_done, 1)

            def low_parts_z(n):
                c, k = divmod(n, KT)
                s = slice(c * NT, (c + 1) * NT)
                dve.wait_ge(z_hi_done, n + 1)
                dve.tensor_tensor(z_lo[:, k, s], z_bank[n % 4][:, :], z_hi[:, k, s].bitcast(F32),
                                  ALU.subtract).then_inc(z_lo_done, 1)

            dve.wait_ge(consts, 2)
            for c in range(CH):
                dve.wait_ge(cond_in[c], GC * DMA)
                gs = slice(c * GC, (c + 1) * GC)
                for q in range(Q):
                    s = slice(q * C, (q + 1) * C)
                    last = dve.tensor_copy(cond_diag[s, gs, q, :], cond_sb[s, gs, :])
                last.then_inc(diag_done, 1)
                if c > 0:
                    for k in range(KT):
                        low_parts_z((c - 1) * KT + k)
            for k in range(KT):
                low_parts_z((CH - 1) * KT + k)

            step = [0]

            def routed(instruction):
                step[0] += 1
                instruction.then_inc(route, 1)
                dve.wait_ge(route, step[0])

            def per_token(n):
                return best[:, n, :].unsqueeze(2).broadcast_to((P, G, E))

            rank_v = rank[:, :].unsqueeze(1).broadcast_to((P, G, E))
            dve.wait_ge(exp_done, 1)
            dve.wait_ge(consts, 3 + E)
            routed(dve.tensor_tensor(prob[:, :, :], logit[:, :, 0:E], logit[:, :, E:2 * E], ALU.add))
            routed(dve.reduce_max(best[:, 0, :], prob[:, :, :], AX_X))
            routed(dve.tensor_tensor(left[:, :, :], prob[:, :, :], per_token(0), ALU.subtract))
            dve.wait_ge(exp_done, 2)
            routed(dve.reduce_sum(best[:, 1, :], prob[:, :, :], AX_X))
            routed(dve.reciprocal(best[:, 2, :], best[:, 1, :]))
            routed(dve.tensor_tensor(prob[:, :, :], prob[:, :, :], per_token(2), ALU.mult))

            def take_best(of, value, mask):
                routed(dve.reduce_max(best[:, value, :], of, AX_X))
                routed(dve.tensor_tensor(pick[:, :, :], of, per_token(value), ALU.is_equal))
                routed(dve.tensor_tensor(pick[:, :, :], pick[:, :, :], rank_v, ALU.mult))
                routed(dve.reduce_max(best[:, 5, :], pick[:, :, :], AX_X))
                routed(dve.tensor_tensor(mask, pick[:, :, :], per_token(5), ALU.is_equal))

            take_best(prob[:, :, :], 3, first[:, :, :])
            routed(dve.scalar_tensor_tensor(left[:, :, :], first[:, :, :], -2.0, prob[:, :, :],
                                            ALU.mult, ALU.add))
            take_best(left[:, :, :], 4, pick[:, :, :])
            routed(dve.tensor_tensor(first[:, :, :], first[:, :, :], pick[:, :, :], ALU.add))
            routed(dve.tensor_tensor(best[:, 5, :], best[:, 3, :], best[:, 4, :], ALU.add))
            routed(dve.reciprocal(best[:, 5, :], best[:, 5, :]))
            routed(dve.tensor_tensor(first[:, :, :], first[:, :, :], prob[:, :, :], ALU.mult))
            dve.tensor_tensor(comb[:, :, :].rearrange("p e g -> p g e"), first[:, :, :], per_token(5),
                              ALU.mult).then_inc(comb_ready, 1)

            def hidden(c, j):
                t = hid[:, j % 2, :]
                wait_tile(dve, silu_done, c, j)
                wait_tile(dve, up_ready, c, j)
                wait_tile(dve, lo_done, c, j - dist(lambda i: i % 2, j))
                dve.tensor_tensor(t, up_bank[j][:, :], silu_g[:, j % 2, :], ALU.mult).then_inc(su_done, 1)
                wait_tile(dve, su_done, c, j)
                dve.wait_ge(comb_in[j], (c + 1) * (DMA * len(expert_rows[j])))
                dve.tensor_tensor(t, t, comb_bc[:, j, :], ALU.mult).then_inc(hid_done, 1)
                wait_tile(dve, hi_done, c, j)
                dve.tensor_tensor(hid_lo[:, j % HS, :], t, hid_hi[:, j % HS, :].bitcast(F32),
                                  ALU.subtract).then_inc(lo_done, 1)

            def add_x(c):
                for b in range(2):
                    dve.wait_ge(tr_ready, 2 * c + (b + 1))
                    g = x_sb[:, bass.ds(c * GC + 2 * b, 2), :]
                    dve.tensor_tensor(g, ps_s[b][:, :].rearrange("p (g t) -> p g t", g=2), g,
                                      ALU.add).then_inc(add_done, 1)

            for j in range(FT):
                hidden(0, j)
            with dve.Fori(1, CH) as c:
                for j in range(FT):
                    hidden(c, j)
                    if j == 4:
                        add_x(c - 1)
            add_x(CH - 1)

        @block.tensor
        def _(pe):
            for n in range(CH * KT):
                c, k = divmod(n, KT)
                if k == 0:
                    pe.wait_ge(x_in[c], DMA)
                    pe.wait_ge(diag_done, c + 1)
                if n >= 4:
                    pe.wait_ge(z_lo_done, n - 3)
                for i in range(GC):
                    g = c * GC + i
                    last = pe.matmul(z_bank[n % 4][:, i * P:(i + 1) * P], x_sb[:, g, k * P:(k + 1) * P],
                                     cond_diag[:, g, :, :].rearrange("p q d -> p (q d)"),
                                     start=True, stop=True)
                last.then_inc(z_ready, 1)

            pe.wait_ge(wr_done, 1)
            for g in range(G):
                if g % GC == 0:
                    pe.wait_ge(z_lo_done, KT * (g // GC + 1))
                parts = [(z, k) for z in (z_hi, z_lo) for k in range(KT)]
                for m, (z, k) in enumerate(parts):
                    last = pe.matmul(ps_s[0][:, g * 2 * E:(g + 1) * 2 * E], z[:, k, g * P:(g + 1) * P],
                                     wr_parts[:, k, :], start=(m == 0), stop=(m == len(parts) - 1))
            last.then_inc(logit_ready, 1)

            def product(bank_ap, w_hi, w_lo, z_at, done):
                parts = [(w, z, k) for k in range(KT) for w, z in ((w_hi, z_hi), (w_lo, z_hi), (w_hi, z_lo))]
                for m, (w, z, k) in enumerate(parts):
                    last = pe.matmul(bank_ap, w(k), z_at(z, k), start=(m == 0), stop=(m == len(parts) - 1))
                last.then_inc(done, 1)

            def gate_up(c, j):
                fs = slice(j * P, (j + 1) * P)
                back = dist(bank_of, j)
                if j == FT - 1 and not (isinstance(c, int) and c == 0):
                    pe.wait_ge(add_done, 2 * c)
                wait_tile(pe, silu_done, c, j - back)
                product(gate_bank[j][:, :], lambda k: wg_hi[:, k, fs], lambda k: wg_lo[:, k, fs],
                        lambda z, k: z[:, k, bass.ts(c, NT)], gate_ready)
                wait_tile(pe, su_done, c, j - back)
                product(up_bank[j][:, :], lambda k: wu_hi[:, k, fs], lambda k: wu_lo[:, k, fs],
                        lambda z, k: z[:, k, bass.ts(c, NT)], up_ready)

            def down(c, j):
                wait_tile(pe, hi_done, c, j)
                if j == 0 and not (isinstance(c, int) and c == 0):
                    pe.wait_ge(out_t_done, KT * c)
                for k in range(KT):
                    hs = slice(k * P, (k + 1) * P)
                    for w, h, m in ((wd_hi, hid_hi, 0), (wd_lo, hid_hi, 1), (wd_hi, hid_lo, 2)):
                        if k == 0 and m == 2:
                            wait_tile(pe, lo_done, c, j)
                        last = pe.matmul(ps_o[k][:, :], w[:, j, hs], h[:, j % HS, :],
                                         start=(j == 0 and m == 0), stop=(j == FT - 1 and m == 2))
                last.then_inc(down_done, 1)

            def transpose_out(c):
                wait_tile(pe, su_done, c, FT - 1)
                pe.wait_ge(out_t_done, KT * (c + 1))
                for i in range(GC):
                    for k in range(KT):
                        at = (i % 2) * H + k * P
                        last = pe.transpose(ps_s[i // 2][:, at:at + P], out_t[:, k, i * P:(i + 1) * P],
                                            ident[:, :])
                    if i % 2:
                        last.then_inc(tr_ready, 1)

            for j in range(FT):
                if j == 0 or piece_of(j) != piece_of(j - 1):
                    pe.wait_ge(gu_lo_done, piece_of(j) + 1)
                if j == LAG:
                    pe.wait_ge(comb_ready, 1)
                    pe.wait_ge(consts, 4 + E)
                    pe.transpose(ps_s[1][:, 0:P], comb[:, :, :].rearrange("p e g -> p (e g)"),
                                 ident[:, :]).then_inc(comb_t_ready, 1)
                if j == FT - 1:
                    pe.wait_ge(exp_done, 1)
                    pe.wait_ge(comb_t_done, 1)
                gate_up(0, j)
                if j >= LAG:
                    if (j - LAG) % DT == 0:
                        pe.wait_ge(d_lo_done, (j - LAG) // DT + 1)
                    down(0, j - LAG)
            pe.wait_ge(d_lo_done, DP)
            with pe.Fori(1, CH) as c:
                for j in range(FT):
                    gate_up(c, j)
                    if j < LAG:
                        down(c - 1, FT - LAG + j)
                    else:
                        down(c, j - LAG)
                    if j == 3:
                        transpose_out(c - 1)
            for j in range(FT - LAG, FT):
                down(CH - 1, j)
            transpose_out(CH - 1)


def kernel(x, itok_B_1_198, L0_cond_weights, L0_ffn_Wr, L0_ffn_Wg, L0_ffn_Wu, L0_ffn_Wd):
    import numpy as np
    import concourse.bacc as bacc
    from concourse.bass_utils import run_bass_kernel_spmd

    nc = bacc.Bacc("TRN2", target_bir_lowering=False, num_devices=1)
    inputs = dict(x=x, token_id=itok_B_1_198, cond_w=L0_cond_weights, w_router=L0_ffn_Wr,
                  w_gate=L0_ffn_Wg, w_up=L0_ffn_Wu, w_down=L0_ffn_Wd)
    arrays, args = {}, []
    for name, value in inputs.items():
        a = np.ascontiguousarray(value)
        arrays[name] = a
        args.append(nc.dram_tensor(name, a.shape, mybir.dt.from_np(a.dtype), kind="ExternalInput").ap())
    args.append(nc.dram_tensor("out", arrays["x"].shape, F32, kind="ExternalOutput").ap())
    adaln_ffn_kernel(nc, *args)
    result = run_bass_kernel_spmd(nc, [arrays], core_ids=[0])
    return result.results[0]["out"]
```

```python
from contextlib import ExitStack

import concourse.bass as bass
from concourse import mybir

ALU = mybir.AluOpType
ACT = mybir.ActivationFunctionType
AX_X = mybir.AxisListType.X
F32 = mybir.dt.float32
F32R = mybir.dt.float32r
I32 = mybir.dt.int32

P = 128
DMA = 16


def adaln_ffn_kernel(nc, x, token_id, cond_w, w_router, w_gate, w_up, w_down, out):
    B, C, H = x.shape
    S, _, D = cond_w.shape
    E, _, I = w_gate.shape
    TOK = B * D
    F = E * I
    FT = F // P
    KT = H // P
    NT = 512
    CH = TOK // NT
    G = TOK // P
    GC = NT // P
    R = P // CH
    Q = P // C
    assert C == D == 32 and F % P == 0 and H % P == 0 and TOK % NT == 0 and E == 8

    WP = 4
    EP = E // WP
    PF = EP * I
    STAGE = 3
    DT = 3
    DP = -(-FT // DT)
    DSTAGE = 2
    HS = 4
    LAG = 2
    LAG0 = 5
    COMB_AT = 3
    HID = LAG0
    DOWN0 = [max(0, 3 * (j + 1 - LAG0) // 2) for j in range(FT)]
    assert DOWN0[-1] == FT - LAG

    x_v = x.rearrange("(g q) c t -> (q c) g t", q=Q)
    out_v = out.rearrange("(g q) c t -> (q c) g t", q=Q)
    cond_rows = cond_w.rearrange("s c d -> s (c d)")
    wr_v = w_router.rearrange("(k p) e -> p k e", p=P)
    wd_v = w_down.rearrange("e i h -> (e i) h").rearrange("(j p) h -> p j h", p=P)
    comb_dram = nc.dram_tensor("comb_dram", [E * G, P], F32, kind="Internal").ap()
    comb_rows = comb_dram.rearrange("(e g) p -> e (g p)", e=E)

    expert_rows = []
    for j in range(FT):
        rows = []
        for e in range(j * P // I, (j * P + P - 1) // I + 1):
            rows.append((e, max(e * I - j * P, 0), min((e + 1) * I - j * P, P)))
        expert_rows.append(rows)

    def piece_of(j):
        return (j * P + P - 1) // PF

    with ExitStack() as ctx:
        def sb(name, shape, dt=F32):
            return ctx.enter_context(nc.sbuf_tensor(name, shape, dt))

        def two_banks(name):
            return ctx.enter_context(nc.psum_tensor(name, [P, 2, NT], F32))

        def sem(name):
            return ctx.enter_context(nc.semaphore(name))

        x_sb = sb("x_sb", [P, G, H])
        ids = sb("ids", [B, 1], I32)
        row_idx = sb("row_idx", [B, 1], I32)
        cond_diag = sb("cond_diag", [P, G, Q, D])
        z_hi = sb("z_hi", [P, KT, TOK], F32R)
        z_lo = sb("z_lo", [P, KT, TOK], F32R)
        wr_stage = sb("wr_stage", [P, KT, E])
        wr_parts = sb("wr_parts", [P, KT, P], F32R)
        gu_stage = sb("gu_stage", [P, STAGE, 2, KT, PF])
        d_stage = sb("d_stage", [P, DSTAGE, DT, H])
        wg_hi = sb("wg_hi", [P, KT, F], F32R)
        wg_lo = sb("wg_lo", [P, KT, F], F32R)
        wu_hi = sb("wu_hi", [P, KT, F], F32R)
        wu_lo = sb("wu_lo", [P, KT, F], F32R)
        wd_hi = sb("wd_hi", [P, FT, H], F32R)
        wd_lo = sb("wd_lo", [P, FT, H], F32R)
        ident = sb("ident", [P, P])
        fold = sb("fold", [P, CH, E])
        rank = sb("rank", [P, E])
        prob = sb("prob", [P, G, E])
        pick = sb("pick", [P, G, E])
        first = sb("first", [P, G, E])
        left = sb("left", [P, G, E])
        best = sb("best", [P, 6, G])
        comb = sb("comb", [P, E, G])
        comb_t = sb("comb_t", [P, P])
        comb_bc = sb("comb_bc", [P, FT, NT])
        cond_sb = comb_bc[0:B, 0:2, :].rearrange("b s n -> b (s n)")
        cond_dc = comb_bc[0:B, 2:4, :].rearrange("b s (d c) -> b (s d) c", c=C)
        logit_t = comb_bc[:, 4, :]
        silu_g = sb("silu_g", [P, 2, NT])
        hid = sb("hid", [P, HID, NT])
        hid_hi = sb("hid_hi", [P, HS, NT], F32R)
        hid_lo = sb("hid_lo", [P, HS, NT], F32R)
        out_t = sb("out_t", [P, KT, NT])

        ps_g = two_banks("ps_g")
        ps_u = two_banks("ps_u")
        ps_o = two_banks("ps_o")
        ps_s = two_banks("ps_s")
        gate_bank = [ps_s[:, 0, :] if j == FT - 1 else ps_g[:, j % 2, :] for j in range(FT)]
        up_bank = [ps_s[:, 1, :] if j == FT - 1 else ps_u[:, j % 2, :] for j in range(FT)]
        z_bank = [ps_g[:, 0, :], ps_g[:, 1, :], ps_u[:, 0, :], ps_u[:, 1, :]]
        router_bank = [ps_s[:, 0, :], ps_s[:, 1, :], ps_o[:, 0, :], ps_o[:, 1, :]]
        logits = ps_s[:, 0, 0:G * E].rearrange("p (i c e) -> p c i e", i=GC, c=CH)
        comb_bank = ps_s[:, 1, 0:P]
        tr_view = ps_s[:, :, :].rearrange("p k (g t) -> p k g t", g=GC)
        M = D // Q
        cond_t = ps_o[:, 0, :].rearrange("p (m b) -> p m b", m=M)

        ids_in = sem("ids_in")
        x_in = [sem(f"x_in{c}") for c in range(CH)]
        wr_in = sem("wr_in")
        gu_in = [sem(f"gu_in{w}") for w in range(WP)]
        d_in = [sem(f"d_in{w}") for w in range(DP)]
        cond_in = sem("cond_in")
        comb_out = sem("comb_out")
        comb_in = [sem(f"comb_in{j}") for j in range(FT)]
        stored = sem("stored")
        consts = sem("consts")
        idx_done = sem("idx_done")
        dc_act = sem("dc_act")
        dc_dve = sem("dc_dve")
        cond_t_ready = sem("cond_t_ready")
        diag_act = sem("diag_act")
        diag_dve = sem("diag_dve")
        z_ready = sem("z_ready")
        z_hi_done = sem("z_hi_done")
        z_lo_done = sem("z_lo_done")
        wr_hi_done = sem("wr_hi_done")
        wr_done = sem("wr_done")
        gu_hi_done = sem("gu_hi_done")
        gu_lo_done = sem("gu_lo_done")
        d_hi_done = sem("d_hi_done")
        d_lo_done = sem("d_lo_done")
        logit_t_ready = sem("logit_t_ready")
        logit_t_done = sem("logit_t_done")
        logit_ready = sem("logit_ready")
        route = sem("route")
        exp_done = sem("exp_done")
        comb_ready = sem("comb_ready")
        comb_t_ready = sem("comb_t_ready")
        comb_t_done = sem("comb_t_done")
        gate_ready = sem("gate_ready")
        up_ready = sem("up_ready")
        silu_done = sem("silu_done")
        su_done = sem("su_done")
        hid_done = sem("hid_done")
        hi_done = sem("hi_done")
        lo_done = sem("lo_done")
        down_done = sem("down_done")
        sum_ready = sem("sum_ready")
        out_t_done = sem("out_t_done")
        tr_ready = sem("tr_ready")
        add_done = sem("add_done")

        def dist(slot_of, j):
            d = 1
            while slot_of((j - d) % FT) != slot_of(j):
                d += 1
            return d

        def bank_of(j):
            return 2 if j == FT - 1 else j % 2

        def wait_tile(eng, semaphore, c, j):
            if isinstance(c, int):
                if c * FT + j + 1 <= 0:
                    return
            eng.wait_ge(semaphore, c * FT + (j + 1))

        WARM = (13, 5)
        ACT_R = 2

        def columns_first(copy, half, *how):
            ds = slice(half * D // 2, (half + 1) * D // 2)
            src = cond_sb[:, :].rearrange("b (c d) -> b d c", c=C)[:, ds, :]
            return copy(cond_dc[:, ds, :], src, *how)

        first_chunk, other_chunks = slice(0, GC), slice(GC, G)

        def diagonal_blocks(copy, groups, rs, *how):
            for q in range(Q):
                for r in rs:
                    src = cond_t[r * C:(r + 1) * C, :, :].rearrange("c m (g q) -> c q g m", q=Q)
                    dst = cond_diag[q * C:(q + 1) * C, :, q, :].rearrange("c g (m r) -> c r g m", r=Q)
                    last = copy(dst[:, r, groups, :], src[:, q, groups, :], *how)
            return last

        block = ctx.enter_context(nc.Block())

        @block.sync
        def _(sp):
            sp.dma_start(ids[:, :], token_id.rearrange("(b a) -> b a", a=1)).then_inc(ids_in, DMA)
            sp.dma_start(wr_stage[:, :, :], wr_v).then_inc(wr_in, DMA)
            for c in range(CH):
                if c == 1:
                    sp.wait_ge(cond_in, DMA)
                sp.dma_start(x_sb[:, c * GC:(c + 1) * GC, :], x_v[:, c * GC:(c + 1) * GC, :]
                             ).then_inc(x_in[c], DMA)

            def load_gate_up(w):
                if w >= STAGE:
                    sp.wait_ge(gu_hi_done, w - STAGE + 1)
                    sp.wait_ge(gu_lo_done, w - STAGE + 1)
                for n, src in enumerate((w_gate, w_up)):
                    for k in range(KT):
                        dst = gu_stage[:, w % STAGE, n, k, :].rearrange("p (e i) -> p e i", e=EP)
                        sp.dma_start(dst, src[w * EP:(w + 1) * EP, k * P:(k + 1) * P, :]
                                     .rearrange("e p i -> p e i")).then_inc(gu_in[w], DMA)

            def load_down(w):
                if w >= DSTAGE:
                    sp.wait_ge(d_hi_done, w - DSTAGE + 1)
                    sp.wait_ge(d_lo_done, w - DSTAGE + 1)
                n = min(DT, FT - w * DT)
                sp.dma_start(d_stage[:, w % DSTAGE, 0:n, :], wd_v[:, w * DT:w * DT + n, :]
                             ).then_inc(d_in[w], DMA)

            load_gate_up(0)
            load_down(0)
            load_gate_up(1)
            load_gate_up(2)
            load_down(1)
            load_gate_up(3)
            load_down(2)

            def broadcast_comb(c, j):
                for e, lo, hi in expert_rows[j]:
                    sp.dma_start(comb_bc[lo:hi, j, :],
                                 comb_rows[e:e + 1, bass.ts(c, NT)].broadcast_to((hi - lo, NT))
                                 ).then_inc(comb_in[j], DMA)

            sp.wait_ge(comb_t_done, 1)
            sp.dma_start(comb_dram, comb_t[:, :]).then_inc(comb_out, DMA)
            sp.wait_ge(comb_out, DMA)
            for j in range(FT):
                broadcast_comb(0, j)
                if j == 2:
                    load_down(3)
            with sp.Fori(1, CH) as c:
                for j in range(FT):
                    wait_tile(sp, hid_done, c - 1, j)
                    broadcast_comb(c, j)

        @block.gpsimd
        def _(pool):
            pool.memset(ident[:, :], 0.0).then_inc(consts, 1)
            pool.wait_ge(consts, 1)
            pool.affine_select(out=ident[:, :], in_=ident[:, :], compare_op=ALU.not_equal, fill=1.0,
                               base=0, pattern=[[-1, P]], channel_multiplier=1).then_inc(consts, 1)
            pool.memset(fold[:, :, :], 0.0).then_inc(consts, 1)
            for n in range(2):
                pool.wait_ge(consts, 3 + n)
                pool.affine_select(out=fold[:, :, :], in_=fold[:, :, :], compare_op=ALU.not_equal,
                                   fill=1.0, base=-n * E, pattern=[[-R, CH], [-1, E]],
                                   channel_multiplier=1).then_inc(consts, 1)
            pool.wait_ge(idx_done, 1)
            pool.indirect_dma_start(
                out=cond_sb[:, :], out_offset=None, in_=cond_rows,
                in_offset=bass.IndirectOffsetOnAxis(ap=row_idx[:, 0:1], axis=0),
            ).then_inc(cond_in, DMA)
            pool.memset(wr_parts[:, :, 2 * E:P].bitcast(F32), 0.0).then_inc(consts, 1)
            pool.memset(cond_diag[:, :, :, :], 0.0).then_inc(consts, 1)
            for e in range(E):
                pool.memset(rank[:, e:e + 1], float(E - e)).then_inc(consts, 1)

            def low_parts_gate_up(w):
                pool.wait_ge(gu_hi_done, w + 1)
                for n, (hi, lo) in enumerate(((wg_hi, wg_lo), (wu_hi, wu_lo))):
                    s = slice(w * PF, (w + 1) * PF)
                    last = pool.tensor_tensor(lo[:, :, s], gu_stage[:, w % STAGE, n, :, :],
                                              hi[:, :, s].bitcast(F32), ALU.subtract)
                last.then_inc(gu_lo_done, 1)

            def low_parts_down(w):
                n = min(DT, FT - w * DT)
                pool.wait_ge(d_hi_done, w + 1)
                s = slice(w * DT, w * DT + n)
                pool.tensor_tensor(wd_lo[:, s, :], d_stage[:, w % DSTAGE, 0:n, :],
                                   wd_hi[:, s, :].bitcast(F32), ALU.subtract).then_inc(d_lo_done, 1)

            low_parts_gate_up(0)
            for w in range(1, WP):
                low_parts_gate_up(w)
                low_parts_down(w - 1)
            low_parts_down(DP - 1)

        @block.scalar
        def _(act):
            def high_parts_gate_up(w):
                act.wait_ge(gu_in[w], 2 * KT * DMA)
                for n, hi in enumerate((wg_hi, wu_hi)):
                    last = act.activation(hi[:, :, w * PF:(w + 1) * PF], gu_stage[:, w % STAGE, n, :, :],
                                          ACT.Copy)
                last.then_inc(gu_hi_done, 1)

            def high_parts_down(w):
                n = min(DT, FT - w * DT)
                act.wait_ge(d_in[w], DMA)
                act.activation(wd_hi[:, w * DT:w * DT + n, :], d_stage[:, w % DSTAGE, 0:n, :],
                               ACT.Copy).then_inc(d_hi_done, 1)

            def logits_from_psum(c):
                act.wait_ge(logit_t_ready, c + 1)
                act.activation(logit_t[c * R:(c + 1) * R, :], router_bank[c][0:R, :], ACT.Copy
                               ).then_inc(logit_t_done, 1)

            act.wait_ge(wr_in, DMA)
            act.activation(wr_parts[:, :, 0:E], wr_stage[:, :, :], ACT.Copy).then_inc(wr_hi_done, 1)
            act.wait_ge(cond_in, DMA)
            columns_first(act.activation, 0, ACT.Copy).then_inc(dc_act, 1)
            act.wait_ge(consts, 7)
            act.wait_ge(cond_t_ready, 1)
            for groups in (first_chunk, other_chunks):
                diagonal_blocks(act.activation, groups, range(ACT_R), ACT.Copy).then_inc(diag_act, 1)
            for n in range(CH * KT):
                c, k = divmod(n, KT)
                act.wait_ge(z_ready, n + 1)
                act.activation(z_hi[:, k, c * NT:(c + 1) * NT], z_bank[n % 4], ACT.Copy
                               ).then_inc(z_hi_done, 1)
                if n == 3:
                    high_parts_gate_up(0)
                if k == 1 and c >= 1:
                    logits_from_psum(c - 1)
            logits_from_psum(CH - 1)
            high_parts_gate_up(1)
            act.wait_ge(route, 2)
            act.activation(prob[:, :, :], left[:, :, :], ACT.Exp).then_inc(exp_done, 1)
            high_parts_down(0)

            def activate(c, j):
                wait_tile(act, gate_ready, c, j)
                wait_tile(act, su_done, c, j - dist(lambda i: i % 2, j))
                act.activation(silu_g[:, j % 2, :], gate_bank[j], ACT.Silu).then_inc(silu_done, 1)

            def split_high(c, j):
                wait_tile(act, hid_done, c, j)
                wait_tile(act, down_done, c, j - dist(lambda i: i % HS, j))
                act.activation(hid_hi[:, j % HS, :], hid[:, j % HID, :], ACT.Copy).then_inc(hi_done, 1)

            def evacuate(c):
                for k in range(KT):
                    if k < KT - 1:
                        act.wait_ge(sum_ready, (KT - 1) * c + (k + 1))
                    else:
                        wait_tile(act, down_done, c, FT - 1)
                    act.activation(out_t[:, k, :], ps_o[:, k, :], ACT.Copy).then_inc(out_t_done, 1)

            for j in range(LAG0):
                if j == COMB_AT:
                    act.wait_ge(comb_t_ready, 1)
                    act.activation(comb_t[:, :], comb_bank, ACT.Copy).then_inc(comb_t_done, 1)
                activate(0, j)
                if j == 1:
                    high_parts_gate_up(2)
                if j == 2:
                    high_parts_down(1)
            for j in range(LAG0, FT):
                for i in range(DOWN0[j - 1], DOWN0[j]):
                    split_high(0, i)
                activate(0, j)
                if j == 5:
                    high_parts_gate_up(3)
                if j == 6:
                    high_parts_down(2)
                if j == 8:
                    high_parts_down(3)
            for j in range(FT - LAG, FT):
                split_high(0, j)
            with act.Fori(1, CH) as c:
                for j in range(FT):
                    if j == LAG:
                        evacuate(c - 1)
                    activate(c, j)
                    split_high(c, j)
                    if j == 6:
                        act.wait_ge(add_done, KT * c)
                        act.dma_start(out_v[:, bass.ds((c - 1) * GC, GC), :],
                                      x_sb[:, bass.ds((c - 1) * GC, GC), :]).then_inc(stored, DMA)
            evacuate(CH - 1)
            for k in range(KT):
                act.wait_ge(add_done, KT * (CH - 1) + k + 1)
                at = slice((CH - 1) * GC, CH * GC), slice(k * P, (k + 1) * P)
                act.dma_start(out_v[:, at[0], at[1]], x_sb[:, at[0], at[1]]).then_inc(stored, DMA)
            act.wait_ge(stored, (CH - 1 + KT) * DMA)

        @block.vector
        def _(dve):
            dve.wait_ge(ids_in, DMA)
            dve.tensor_scalar(row_idx[:, :], ids[:, :], 0.0, float(S - 1), ALU.max, ALU.min
                              ).then_inc(idx_done, 1)
            dve.wait_ge(wr_hi_done, 1)
            dve.tensor_tensor(wr_parts[:, :, E:2 * E], wr_stage[:, :, :],
                              wr_parts[:, :, 0:E].bitcast(F32), ALU.subtract).then_inc(wr_done, 1)

            def low_parts_z(n):
                c, k = divmod(n, KT)
                s = slice(c * NT, (c + 1) * NT)
                dve.wait_ge(z_hi_done, n + 1)
                dve.tensor_tensor(z_lo[:, k, s], z_bank[n % 4], z_hi[:, k, s].bitcast(F32),
                                  ALU.subtract).then_inc(z_lo_done, 1)

            dve.wait_ge(cond_in, DMA)
            columns_first(dve.tensor_copy, 1).then_inc(dc_dve, 1)
            dve.wait_ge(consts, 7)
            dve.wait_ge(cond_t_ready, 1)
            for groups in (first_chunk, other_chunks):
                diagonal_blocks(dve.tensor_copy, groups, range(ACT_R, Q)).then_inc(diag_dve, 1)
            for n in range(CH * KT):
                low_parts_z(n)

            def gated(c, j):
                t = hid[:, j % HID, :]
                wait_tile(dve, silu_done, c, j)
                wait_tile(dve, up_ready, c, j)
                wait_tile(dve, lo_done, c, j - dist(lambda i: i % HID, j))
                dve.tensor_tensor(t, up_bank[j], silu_g[:, j % 2, :], ALU.mult).then_inc(su_done, 1)

            def combined(c, j):
                t = hid[:, j % HID, :]
                wait_tile(dve, su_done, c, j)
                dve.wait_ge(comb_in[j], (c + 1) * (DMA * len(expert_rows[j])))
                dve.tensor_tensor(t, t, comb_bc[:, j, :], ALU.mult).then_inc(hid_done, 1)
                wait_tile(dve, hi_done, c, j)
                dve.tensor_tensor(hid_lo[:, j % HS, :], t, hid_hi[:, j % HS, :].bitcast(F32),
                                  ALU.subtract).then_inc(lo_done, 1)

            step = [0]

            def routed(instruction):
                step[0] += 1
                instruction.then_inc(route, 1)
                dve.wait_ge(route, step[0])

            def per_token(n):
                return best[:, n, :].unsqueeze(2).broadcast_to((P, G, E))

            def by_chunk(t):
                return t.rearrange("p (c i) e -> p c i e", c=CH)

            rank_v = rank[:, :].unsqueeze(1).broadcast_to((P, G, E))
            dve.wait_ge(logit_ready, 1)
            dve.wait_ge(consts, 7 + E)
            routed(dve.reduce_max(best[:, 0, :].rearrange("p (c i) -> p c i", c=CH), logits, AX_X))
            routed(dve.tensor_tensor(by_chunk(left[:, :, :]), logits, by_chunk(per_token(0)), ALU.subtract))
            dve.wait_ge(exp_done, 1)
            routed(dve.reduce_sum(best[:, 1, :], prob[:, :, :], AX_X))
            routed(dve.reciprocal(best[:, 2, :], best[:, 1, :]))
            routed(dve.tensor_tensor(prob[:, :, :], prob[:, :, :], per_token(2), ALU.mult))

            def take_best(of, value, mask):
                routed(dve.reduce_max(best[:, value, :], of, AX_X))
                routed(dve.tensor_tensor(pick[:, :, :], of, per_token(value), ALU.is_equal))
                routed(dve.tensor_tensor(pick[:, :, :], pick[:, :, :], rank_v, ALU.mult))
                routed(dve.reduce_max(best[:, 5, :], pick[:, :, :], AX_X))
                routed(dve.tensor_tensor(mask, pick[:, :, :], per_token(5), ALU.is_equal))

            take_best(prob[:, :, :], 3, first[:, :, :])
            routed(dve.scalar_tensor_tensor(left[:, :, :], first[:, :, :], -2.0, prob[:, :, :],
                                            ALU.mult, ALU.add))
            gated(0, 0)
            take_best(left[:, :, :], 4, pick[:, :, :])
            routed(dve.tensor_tensor(first[:, :, :], first[:, :, :], pick[:, :, :], ALU.add))
            routed(dve.tensor_tensor(best[:, 5, :], best[:, 3, :], best[:, 4, :], ALU.add))
            routed(dve.reciprocal(best[:, 5, :], best[:, 5, :]))
            routed(dve.tensor_tensor(first[:, :, :], first[:, :, :], prob[:, :, :], ALU.mult))
            dve.tensor_tensor(comb[:, :, :].rearrange("p e g -> p g e"), first[:, :, :], per_token(5),
                              ALU.mult).then_inc(comb_ready, 1)

            def add_x(c):
                for k in range(KT):
                    dve.wait_ge(tr_ready, KT * c + (k + 1))
                    at = x_sb[:, bass.ds(c * GC, GC), k * P:(k + 1) * P]
                    dve.tensor_tensor(at, tr_view[:, k, :, :], at, ALU.add).then_inc(add_done, 1)

            for j in range(1, LAG0):
                gated(0, j)
            for j in range(LAG0, FT):
                for i in range(DOWN0[j - 1], DOWN0[j]):
                    combined(0, i)
                gated(0, j)
            for j in range(FT - LAG, FT):
                combined(0, j)
            with dve.Fori(1, CH) as c:
                for j in range(FT):
                    gated(c, j)
                    combined(c, j)
                    if j == 4:
                        add_x(c - 1)
            add_x(CH - 1)

        @block.tensor
        def _(pe):
            def keep_warm(n):
                for _ in range(n):
                    pe.matmul(ps_s[:, 0, 0:P], ident[:, :], ident[:, :], start=True, stop=True)

            pe.wait_ge(consts, 2)
            keep_warm(WARM[0])
            pe.wait_ge(dc_act, 1)
            pe.wait_ge(dc_dve, 1)
            for m in range(M):
                last = pe.matmul(cond_t[:, m, :], cond_dc[:, m * Q:(m + 1) * Q, :].rearrange("b r c -> b (r c)"),
                                 ident[0:B, 0:B], start=True, stop=True)
            last.then_inc(cond_t_ready, 1)

            keep_warm(WARM[1])

            def z_tiles(c):
                pe.wait_ge(x_in[c], DMA)
                if c < 2:
                    pe.wait_ge(diag_act, c + 1)
                    pe.wait_ge(diag_dve, c + 1)
                for k in range(KT):
                    n = c * KT + k
                    if n >= 4:
                        pe.wait_ge(z_lo_done, n - 3)
                    for i in range(GC):
                        g = c * GC + i
                        last = pe.matmul(z_bank[n % 4][:, i * P:(i + 1) * P], x_sb[:, g, k * P:(k + 1) * P],
                                         cond_diag[:, g, :, :].rearrange("p q d -> p (q d)"),
                                         start=True, stop=True)
                    last.then_inc(z_ready, 1)

            def router(c):
                parts = [(z, k) for z in (z_hi, z_lo) for k in range(KT)]
                for m, (z, k) in enumerate(parts):
                    if k == 0:
                        pe.wait_ge(z_hi_done if z is z_hi else z_lo_done, KT * (c + 1))
                    last = pe.matmul(router_bank[c], wr_parts[:, k, :], z[:, k, c * NT:(c + 1) * NT],
                                     start=(m == 0), stop=(m == len(parts) - 1))
                last.then_inc(logit_t_ready, 1)

            def fold_logits():
                pe.wait_ge(logit_t_done, CH)
                for i in range(GC):
                    last = pe.matmul(ps_s[:, 0, i * CH * E:(i + 1) * CH * E], logit_t[:, i * P:(i + 1) * P],
                                     fold[:, :, :].rearrange("p c e -> p (c e)"), start=True, stop=True)
                last.then_inc(logit_ready, 1)

            def transpose_comb():
                pe.wait_ge(comb_ready, 1)
                pe.transpose(comb_bank, comb[:, :, :].rearrange("p e g -> p (e g)"), ident[:, :]
                             ).then_inc(comb_t_ready, 1)

            z_tiles(0)
            pe.wait_ge(wr_done, 1)
            pe.wait_ge(consts, 7)
            for c in range(1, CH):
                z_tiles(c)
                router(c - 1)
            router(CH - 1)

            def product(bank_ap, w_hi, w_lo, z_at, done):
                parts = [(w, z, k) for k in range(KT) for w, z in ((w_hi, z_hi), (w_hi, z_lo), (w_lo, z_hi))]
                for m, (w, z, k) in enumerate(parts):
                    last = pe.matmul(bank_ap, w(k), z_at(z, k), start=(m == 0), stop=(m == len(parts) - 1))
                last.then_inc(done, 1)

            def gate_up(c, j, between=None):
                fs = slice(j * P, (j + 1) * P)
                back = dist(bank_of, j)
                if j == FT - 1 and not (isinstance(c, int) and c == 0):
                    pe.wait_ge(add_done, KT * c)
                wait_tile(pe, silu_done, c, j - back)
                product(gate_bank[j], lambda k: wg_hi[:, k, fs], lambda k: wg_lo[:, k, fs],
                        lambda z, k: z[:, k, bass.ts(c, NT)], gate_ready)
                if between:
                    between()
                wait_tile(pe, su_done, c, j - back)
                product(up_bank[j], lambda k: wu_hi[:, k, fs], lambda k: wu_lo[:, k, fs],
                        lambda z, k: z[:, k, bass.ts(c, NT)], up_ready)

            def down(c, j):
                wait_tile(pe, hi_done, c, j)
                if j == 0 and not (isinstance(c, int) and c == 0):
                    pe.wait_ge(out_t_done, KT * c)
                for k in range(KT):
                    hs = slice(k * P, (k + 1) * P)
                    for w, h, m in ((wd_hi, hid_hi, 0), (wd_lo, hid_hi, 1), (wd_hi, hid_lo, 2)):
                        if k == 0 and m == 2:
                            wait_tile(pe, lo_done, c, j)
                        last = pe.matmul(ps_o[:, k, :], w[:, j, hs], h[:, j % HS, :],
                                         start=(j == 0 and m == 0), stop=(j == FT - 1 and m == 2))
                    if j == FT - 1 and k < KT - 1:
                        last.then_inc(sum_ready, 1)
                last.then_inc(down_done, 1)

            def transpose_out(c):
                wait_tile(pe, su_done, c, FT - 1)
                for k in range(KT):
                    pe.wait_ge(out_t_done, KT * c + (k + 1))
                    for i in range(GC):
                        last = pe.transpose(tr_view[:, k, i, :], out_t[:, k, i * P:(i + 1) * P],
                                            ident[:, :])
                    last.then_inc(tr_ready, 1)

            for j in range(FT):
                if j == 0 or piece_of(j) != piece_of(j - 1):
                    pe.wait_ge(gu_lo_done, piece_of(j) + 1)
                if j == FT - 1:
                    pe.wait_ge(comb_t_done, 1)
                gate_up(0, j, between={0: fold_logits, COMB_AT: transpose_comb}.get(j))
                for i in range(DOWN0[j - 1] if j else 0, DOWN0[j]):
                    if i % DT == 0:
                        pe.wait_ge(d_lo_done, i // DT + 1)
                    down(0, i)
            pe.wait_ge(d_lo_done, DP)
            with pe.Fori(1, CH) as c:
                for j in range(FT):
                    gate_up(c, j)
                    if j < LAG:
                        down(c - 1, FT - LAG + j)
                    else:
                        down(c, j - LAG)
                    if j == 3:
                        transpose_out(c - 1)
            for j in range(FT - LAG, FT):
                down(CH - 1, j)
            transpose_out(CH - 1)


def kernel(x, itok_B_1_198, L0_cond_weights, L0_ffn_Wr, L0_ffn_Wg, L0_ffn_Wu, L0_ffn_Wd):
    import numpy as np
    import concourse.bacc as bacc
    from concourse.bass_utils import run_bass_kernel_spmd

    nc = bacc.Bacc("TRN2", target_bir_lowering=False, num_devices=1)
    inputs = dict(x=x, token_id=itok_B_1_198, cond_w=L0_cond_weights, w_router=L0_ffn_Wr,
                  w_gate=L0_ffn_Wg, w_up=L0_ffn_Wu, w_down=L0_ffn_Wd)
    arrays, args = {}, []
    for name, value in inputs.items():
        a = np.ascontiguousarray(value)
        arrays[name] = a
        args.append(nc.dram_tensor(name, a.shape, mybir.dt.from_np(a.dtype), kind="ExternalInput").ap())
    args.append(nc.dram_tensor("out", arrays["x"].shape, F32, kind="ExternalOutput").ap())
    adaln_ffn_kernel(nc, *args)
    result = run_bass_kernel_spmd(nc, [arrays], core_ids=[0])
    return result.results[0]["out"]
```
